# Optimizing a Trainium2 kernel written in Bass

```python
import numpy as np
import jax
import jax.numpy as jnp

def _softmax(x, axis=-1):
    return jax.nn.softmax(x, axis=axis)
def _gelu(x):
    return jax.nn.gelu(x, approximate=True)
def _silu(x):
    return jax.nn.silu(x)
def _sigmoid(x):
    return jax.nn.sigmoid(x)
def _layernorm(x, axis=-1, eps=1e-5):
    m = jnp.mean(x, axis=axis, keepdims=True)
    v = jnp.var(x, axis=axis, keepdims=True)
    return (x - m) / jnp.sqrt(v + eps)
def _scatter_add(tgt, idx, src, axis=0):
    return tgt.at[idx].add(src)
def _segment_sum(src, seg, n):
    return jax.ops.segment_sum(src, seg, n)

kernel_name = 'mk_conv_preact_d1_conv_nchw768_a461b6'

def setup_inputs(seed: int = 0):
    np.random.seed(seed)
    _w = jnp.asarray
    def _rec_inputs():
        import jax
        import jax.numpy as jnp
        _gk = jax.random.key(seed)
        x = -0.0001538 + 1 * jax.random.normal(jax.random.fold_in(_gk, 1), (8, 768, 32, 32), jnp.float32)
        return x
    x = _rec_inputs()
    def _L0_conv_setup():
        import jax, jax.numpy as jnp
        import numpy as np
        HEADS = 12
        key = jax.random.key(seed)
        ks = jax.random.split(key, 5)
        B, C, H, W = (8, 768, 32, 32)
        s = 1.0 / np.sqrt(C)
        x = jax.random.normal(ks[0], (B, C, H, W), dtype=jnp.float32)
        Wq = jax.random.normal(ks[1], (C, C), dtype=jnp.float32) * s
        Wk = jax.random.normal(ks[2], (C, C), dtype=jnp.float32) * s
        Wv = jax.random.normal(ks[3], (C, C), dtype=jnp.float32) * s
        Wp = jax.random.normal(ks[4], (C, C), dtype=jnp.float32) * s
        return {'x': x, 'Wq': Wq, 'Wk': Wk, 'Wv': Wv, 'Wp': Wp}
    _L0_conv_all = _L0_conv_setup()
    _L0_conv_in = {k: v for k, v in _L0_conv_all.items() if k in ('Wq', 'Wk', 'Wv', 'Wp', )}
    del _L0_conv_all

    return {
        "x": x,
        "L0_conv_Wq": _L0_conv_in["Wq"],
        "L0_conv_Wk": _L0_conv_in["Wk"],
        "L0_conv_Wv": _L0_conv_in["Wv"],
        "L0_conv_Wp": _L0_conv_in["Wp"],
    }

def reference(x, L0_conv_Wq, L0_conv_Wk, L0_conv_Wv, L0_conv_Wp):
    import jax
    import jax.numpy as jnp
    def _L0_conv_ref(x, Wq, Wk, Wv, Wp):
        import jax, jax.numpy as jnp
        import numpy as np
        HEADS = 12
        B, C, H, W = x.shape
        h = HEADS
        dh = C // h
        N = H * W

        def conv1x1(Wm):
            y = jnp.einsum('oc,bchw->bohw', Wm, x)
            return y.reshape(B, h, dh, N)
        q = conv1x1(Wq)
        k = conv1x1(Wk)
        v = conv1x1(Wv)
        scale = 1.0 / jnp.sqrt(jnp.asarray(dh, dtype=x.dtype))
        scores = jnp.einsum('bhdn,bhdm->bhnm', q, k) * scale
        attn = jax.nn.softmax(scores, axis=-1)
        out = jnp.einsum('bhnm,bhdm->bhdn', attn, v)
        out = out.reshape(B, C, H, W)
        return jnp.einsum('oc,bchw->bohw', Wp, out)

    def _gn(v, G=32, eps=1e-5):
        B_, C_, H_, W_ = v.shape
        g = v.reshape(B_, G, C_ // G, H_, W_)
        m = jnp.mean(g, axis=(2, 3, 4), keepdims=True)
        s = jnp.var(g, axis=(2, 3, 4), keepdims=True)
        return ((g - m) / jnp.sqrt(s + eps)).reshape(v.shape)

    def _ln_c(v, eps=1e-6):
        m = jnp.mean(v, axis=1, keepdims=True)
        s = jnp.var(v, axis=1, keepdims=True)
        return (v - m) / jnp.sqrt(s + eps)

    def _ln_t(v, eps=1e-5):
        m = jnp.mean(v, axis=-1, keepdims=True)
        s = jnp.var(v, axis=-1, keepdims=True)
        return (v - m) / jnp.sqrt(s + eps)

    def _to_tokens(v):
        B_, C_, H_, W_ = v.shape
        return v.reshape(B_, C_, H_ * W_).transpose(0, 2, 1)
    def _from_tokens(t, like):
        B_, C_, H_, W_ = like.shape
        return t.transpose(0, 2, 1).reshape(B_, C_, H_, W_)

    x = x + _L0_conv_ref(_gn(x), L0_conv_Wq, L0_conv_Wk, L0_conv_Wv, L0_conv_Wp)
    return x


_drawn_inputs = setup_inputs


def setup_inputs(seed=0):
    import zlib

    import numpy as np

    out = dict(_drawn_inputs(seed))
    spreads = {}
    factors = {}
    for name, (base, spread) in spreads.items():
        noise = np.random.default_rng([zlib.crc32(name.encode()), seed]).standard_normal(out[name].shape)
        drawn = base * np.exp(spread * noise) if base else spread * noise
        out[name] = jnp.asarray(drawn.astype(out[name].dtype))
    for name, factor in factors.items():
        out[name] = (out[name] * factor).astype(out[name].dtype)
    return out
```

```python
from contextlib import ExitStack

import concourse.bass as bass
from concourse import mybir

F32 = mybir.dt.float32
F32R = mybir.dt.float32r
I32 = mybir.dt.int32
ALU = mybir.AluOpType
ACT = mybir.ActivationFunctionType
AX = mybir.AxisListType

P = 128
BANK = 512
HEADS = 12
GROUPS = 32
EPS = 1e-5


def f32(ap):
    return ap.bitcast(F32)


class Shapes:
    def __init__(self, x):
        self.B, self.C, self.N = x.shape
        self.KT = self.C // P
        self.DH = self.C // HEADS
        self.HALVES = self.N // BANK
        self.MT = self.N // P
        self.NH = self.B * HEADS


def project_phase(nc, S, x, weights, ident_in, avg_in, wp_dram, q_dram, k_dram, v_dram, psum):
    B, C, N, KT, DH = S.B, S.C, S.N, S.KT, S.DH
    TP = 3
    WG = KT * KT // TP
    VC = C // 2
    VH = VC // DH
    NT = BANK // P
    RING = 4
    PER_HALF = 2 * KT + 2 * NT
    NCH = C * N // P // BANK
    assert PER_HALF % RING == 0

    with ExitStack() as ctx:
        def sb(name, shape, dt=F32):
            return ctx.enter_context(nc.sbuf_tensor(name, shape, dt))

        def sem(name):
            return ctx.enter_context(nc.semaphore(name))

        w_hi = sb("w_hi", [P, 3, KT, C], F32R)
        w_lo = sb("w_lo", [P, 3, KT, C], F32R)
        x_raw = sb("x_raw", [P, KT, N])
        w_nat = x_raw[:, :, 0:C]
        xn = sb("xn", [P, 2, BANK])
        xn_hi = sb("xn_hi", [P, 2, KT, BANK], F32R)
        xn_lo = sb("xn_lo", [P, 2, KT, BANK], F32R)
        stage = sb("stage", [P, RING, 2 * BANK], F32R)
        ident = sb("ident_a", [P, P])
        wp_hi = xn_hi[:, :, :, :].rearrange("p a k n -> p (a k n)")[:, 0:KT * C].rearrange("p (k o) -> p k o", k=KT)
        wp_lo = xn_lo[:, :, :, :].rearrange("p a k n -> p (a k n)")[:, 0:KT * C].rearrange("p (k o) -> p k o", k=KT)
        avg = sb("avg", [P, P])
        stats = sb("stats", [P, NCH, 6])
        mom = sb("mom", [P, 2])
        mean = sb("mean", [P, 1])
        dev = sb("dev", [P, 1])
        spread = sb("spread", [P, 1])
        var = sb("var", [P, 1])
        yi = sb("yi", [P, 1], I32)
        yf = sb("yf", [P, 1])
        rs = sb("rs", [P, 1])
        t0 = sb("t0", [P, 1])
        t1 = sb("t1", [P, 1])
        shift = sb("shift", [P, 1])

        const_in = sem("const_in")
        w_in = sem("w_in")
        w_turned = sem("w_turned")
        w_hi_done = sem("w_hi_done")
        w_lo_done = sem("w_lo_done")
        wp_out = sem("wp_out")
        x_in = sem("x_in")
        stats_step = sem("stats_step")
        bn_done = sem("bn_done")
        mean_ps = sem("mean_ps")
        dev_done = sem("dev_done")
        var_ps = sem("var_ps")
        norm_done = sem("norm_done")
        xn_made = sem("xn_made")
        xn_hi_done = sem("xn_hi_done")
        xn_lo_done = sem("xn_lo_done")
        group_done = sem("group_done")
        hi_done = sem("hi_done")
        lo_done = sem("lo_done")
        stored = [sem(f"stored{r}") for r in range(RING)]


        x_v = x.rearrange("b (p k) n -> b p k n", k=KT)

        CHAIN = 5 + 3 * 4 + 1
        NEXT_AT = (0, 2)
        STATS_AT, AGGREGATE_AT = 11, 17

        def known(n):
            return isinstance(n, int)

        def wait(eng, s, n):
            if not (known(n) and n <= 0):
                eng.wait_ge(s, n)

        STORES = [sum(2 if g < 2 * KT else 1 for g in range(r, PER_HALF, RING)) for r in range(RING)]

        def stored_before(unit, g):
            r = g % RING
            return 16 * (unit * STORES[r] + sum(2 if h < 2 * KT else 1 for h in range(r, g, RING)))

        def all_batches(eng, batch):
            batch(0, False)
            with eng.Fori(1, B - 1) as b:
                batch(b, False)
            batch(B - 1, True)

        def prepared(half, g):
            kt = g - NEXT_AT[half]
            return kt if 0 <= kt < KT else None

        block = ctx.enter_context(nc.Block())

        @block.sync
        def _(sp):
            sp.dma_start(ident[:], ident_in).then_inc(const_in, 16)
            sp.dma_start(avg[:], avg_in).then_inc(const_in, 16)
            for w in range(4):
                if w >= 1:
                    sp.wait_ge(w_turned, w * WG)
                sp.dma_start(w_nat, weights[w].rearrange("(o p) c -> p o c", p=P)).then_inc(w_in, 16)
                if w == 1:
                    sp.wait_ge(w_lo_done, WG)
                    for part, src in enumerate((wp_hi, wp_lo)):
                        sp.dma_start(wp_dram[part].rearrange("(k p) o -> p k o", p=P), f32(src)).then_inc(wp_out, 16)
            sp.wait_ge(w_turned, 4 * WG)
            sp.dma_start(x_raw[:], x_v[0]).then_inc(x_in, 16)

            def batch(b, last):
                for half in range(S.HALVES):
                    for g in range(PER_HALF):
                        r = g % RING
                        if half == 0 and g == NEXT_AT[0] + KT and not last:
                            sp.wait_ge(xn_made, (b + 1) * S.HALVES * KT)
                            sp.dma_start(x_raw[:], x_v[bass.ds(b + 1, 1)]).then_inc(x_in, 16)
                        sp.wait_ge(lo_done, (b * S.HALVES + half) * PER_HALF + g + 1)
                        if g < 2 * KT:
                            dst = q_dram if g < KT else k_dram
                            rows = bass.ds(b * C + g % KT * P, P)
                            for part in range(2):
                                sp.dma_start(dst[part, rows, half * BANK:(half + 1) * BANK],
                                             f32(stage[:, r, part * BANK:(part + 1) * BANK])).then_inc(stored[r], 16)
                        else:
                            nt, cg = (g - 2 * KT) // 2, (g - 2 * KT) % 2
                            sp.dma_start(v_dram[bass.ds(b * HEADS + cg * VH, VH), :, half * NT + nt, :].rearrange("h p d -> p h d"),
                                         f32(stage[:, r, 0:2 * VC]).rearrange("p (h d) -> p h d", h=VH)).then_inc(stored[r], 16)

            all_batches(sp, batch)
            sp.wait_ge(wp_out, 32)
            for r in range(RING):
                sp.wait_ge(stored[r], 16 * STORES[r] * S.HALVES * B)

        @block.tensor
        def _(pe):
            pe.wait_ge(const_in, 32)
            for w in range(4):
                pe.wait_ge(w_in, 16 * (w + 1))
                for g in range(WG):
                    n = w * WG + g
                    wait(pe, w_lo_done, n - RING + 1)
                    kt, o0 = g // (KT // TP), g % (KT // TP) * TP
                    src = w_nat.rearrange("p o (k c) -> p o k c", k=KT) if w == 0 else \
                        w_nat.rearrange("p o (c k) -> p o k c", k=KT)
                    for o in range(TP):
                        mm = pe.transpose(psum[:, n % RING, o * P:(o + 1) * P], src[:, o0 + o, kt, :], ident[:])
                    mm.then_inc(w_turned, 1)

            def mean_product(b):
                pe.wait_ge(stats_step, CHAIN * b + 1)
                pe.matmul(psum[:, RING, 0:1], avg[:], mom[:, 0:1], start=True, stop=True).then_inc(mean_ps, 1)

            def variance_product(b):
                pe.wait_ge(dev_done, b + 1)
                pe.matmul(psum[:, RING + 1, 0:1], avg[:], spread[:], start=True, stop=True).then_inc(var_ps, 1)

            def project(b, half, last):
                unit = b * S.HALVES + half
                for g in range(PER_HALF):
                    r = g % RING
                    wait(pe, lo_done, unit * PER_HALF + g - RING + 1)
                    out = psum[:, r, :]
                    for kt in range(KT):
                        if g == 0:
                            pe.wait_ge(xn_lo_done, unit * KT + kt + 1)
                        a, z = xn_hi[:, half, kt, :], xn_lo[:, half, kt, :]
                        if g < 2 * KT:
                            w, cols = g // KT, slice(g % KT * P, (g % KT + 1) * P)
                            wa, wz = w_hi[:, w, kt, cols], w_lo[:, w, kt, cols]
                            parts = [(wa, a), (wa, z), (wz, a)]
                        else:
                            nt, cg = (g - 2 * KT) // 2, (g - 2 * KT) % 2
                            t, cols = slice(nt * P, (nt + 1) * P), slice(cg * VC, (cg + 1) * VC)
                            va, vz = w_hi[:, 2, kt, cols], w_lo[:, 2, kt, cols]
                            parts = [(a[:, t], va), (a[:, t], vz), (z[:, t], va)]
                            out = psum[:, r, 0:VC]
                        for n, (lhs, rhs) in enumerate(parts):
                            mm = pe.matmul(out, lhs, rhs, start=(kt == 0 and n == 0), stop=(kt == KT - 1 and n == 2))
                    mm.then_inc(group_done, 1)
                    if half == 0 and not last:
                        if g == AGGREGATE_AT + 1:
                            mean_product(b + 1)
                        if g == AGGREGATE_AT + 2:
                            variance_product(b + 1)

            mean_product(0)
            variance_product(0)

            def batch(b, last):
                project(b, 0, last)
                project(b, 1, last)

            all_batches(pe, batch)

        @block.scalar
        def _(act):
            for n in range(4 * WG):
                w, g = n // WG, n % WG
                kt, o0 = g // (KT // TP), g % (KT // TP) * TP
                cols = slice(o0 * P, (o0 + TP) * P)
                act.wait_ge(w_turned, n + 1)
                act.copy((wp_hi if w == 0 else w_hi[:, w - 1])[:, kt, cols], psum[:, n % RING, 0:TP * P]).then_inc(w_hi_done, 1)

            def normalise(unit, half, kt):
                wait(act, xn_lo_done, unit * KT + kt - 1)
                act.activation(xn[:, kt % 2, :], x_raw[:, kt, half * BANK:(half + 1) * BANK], ACT.Identity,
                               bias=shift[:, 0:1], scale=rs[:, 0:1]).then_inc(xn_made, 1)

            act.wait_ge(norm_done, 1)
            for kt in range(KT):
                normalise(0, 0, kt)

            def batch(b, last):
                for half in range(S.HALVES):
                    unit = b * S.HALVES + half
                    for g in range(PER_HALF):
                        r = g % RING
                        act.wait_ge(group_done, unit * PER_HALF + g + 1)
                        wait(act, stored[r], stored_before(unit, g))
                        if g < 2 * KT:
                            dst, src = stage[:, r, 0:BANK], psum[:, r, :]
                        else:
                            dst = stage[:, r, 0:2 * VC].rearrange("p (h s d) -> p h s d", h=VH, s=2)[:, :, 0, :]
                            src = psum[:, r, 0:VC].rearrange("p (h d) -> p h d", h=VH)
                        act.copy(dst, src).then_inc(hi_done, 1)
                        kt = prepared(half, g)
                        if kt is not None and not (last and half == 1):
                            if half == 1 and kt == 0:
                                act.wait_ge(norm_done, b + 2)
                            normalise(unit + 1, 1 - half, kt)

            all_batches(act, batch)

        @block.vector
        def _(dve):
            for n in range(4 * WG):
                w, g = n // WG, n % WG
                kt, o0 = g // (KT // TP), g % (KT // TP) * TP
                cols = slice(o0 * P, (o0 + TP) * P)
                hi, lo = (wp_hi, wp_lo) if w == 0 else (w_hi[:, w - 1], w_lo[:, w - 1])
                dve.wait_ge(w_hi_done, n + 1)
                dve.tensor_tensor(lo[:, kt, cols], psum[:, n % RING, 0:TP * P], f32(hi[:, kt, cols]),
                                  ALU.subtract).then_inc(w_lo_done, 1)

            def link(op, b, n):
                op.then_inc(stats_step, 1)
                dve.wait_ge(stats_step, CHAIN * b + n)

            def chunk(b, c):
                if c == 0:
                    dve.wait_ge(x_in, 16 * (b + 1))
                kt, h = c // S.HALVES, c % S.HALVES
                op = dve.bn_stats(stats[:, c, :], x_raw[:, kt, h * BANK:(h + 1) * BANK])
                if c == NCH - 1:
                    op.then_inc(bn_done, 1)

            def aggregate(b):
                dve.wait_ge(bn_done, b + 1)
                dve.tensor_copy(t0[:], stats[:, 0, 0:1])
                dve.bn_aggr(mom[:], stats[:]).then_inc(stats_step, 1)

            def deviation(b):
                dve.wait_ge(mean_ps, b + 1)
                link(dve.tensor_copy(mean[:], psum[:, RING, 0:1]), b, 2)
                link(dve.tensor_tensor(dev[:], mom[:, 0:1], mean[:], ALU.subtract), b, 3)
                dve.scalar_tensor_tensor(spread[:], dev[:], dev[:, 0:1], mom[:, 1:2], ALU.mult, ALU.add).then_inc(dev_done, 1)

            def inverse_root(b):
                dve.wait_ge(var_ps, b + 1)
                link(dve.tensor_scalar(var[:], psum[:, RING + 1, 0:1], EPS, None, ALU.add), b, 4)
                link(dve.tensor_scalar(yi[:], var[:].bitcast(I32), 1, None, ALU.arith_shift_right), b, 5)
                wait(dve, xn_made, b * S.HALVES * KT)
                link(dve.tensor_scalar(rs[:].bitcast(I32), yi[:], -1.0, float(0x5F3759DF), ALU.mult, ALU.add), b, 6)
                for n in range(4):
                    link(dve.scalar_tensor_tensor(t0[:], rs[:], rs[:, 0:1], var[:], ALU.mult, ALU.mult), b, 7 + 3 * n)
                    link(dve.tensor_scalar(t1[:], t0[:], -0.5, 1.5, ALU.mult, ALU.add), b, 8 + 3 * n)
                    link(dve.tensor_tensor(rs[:], rs[:], t1[:], ALU.mult), b, 9 + 3 * n)
                dve.scalar_tensor_tensor(shift[:], mean[:], -1.0, rs[:], ALU.mult, ALU.mult).then_inc(norm_done, 1)

            def split_x(unit, half, kt):
                n = unit * KT + kt + 1
                if kt == 0:
                    wait(dve, group_done, (unit - 1) * PER_HALF)
                dve.wait_ge(xn_made, n)
                dve.tensor_copy(xn_hi[:, half, kt, :], xn[:, kt % 2, :]).then_inc(xn_hi_done, 1)
                dve.wait_ge(xn_hi_done, n)
                dve.tensor_tensor(xn_lo[:, half, kt, :], xn[:, kt % 2, :], f32(xn_hi[:, half, kt, :]),
                                  ALU.subtract).then_inc(xn_lo_done, 1)

            for c in range(NCH):
                chunk(0, c)
            aggregate(0)
            deviation(0)
            inverse_root(0)
            dve.wait_ge(wp_out, 32)
            for kt in range(KT):
                split_x(0, 0, kt)

            def batch(b, last):
                for half in range(S.HALVES):
                    unit = b * S.HALVES + half
                    for g in range(PER_HALF):
                        r = g % RING
                        dve.wait_ge(hi_done, unit * PER_HALF + g + 1)
                        if g < 2 * KT:
                            dve.tensor_tensor(stage[:, r, BANK:2 * BANK], psum[:, r, :], f32(stage[:, r, 0:BANK]),
                                              ALU.subtract).then_inc(lo_done, 1)
                        else:
                            both = stage[:, r, 0:2 * VC].rearrange("p (h s d) -> p h s d", h=VH, s=2)
                            dve.tensor_tensor(both[:, :, 1, :], psum[:, r, 0:VC].rearrange("p (h d) -> p h d", h=VH),
                                              f32(both[:, :, 0, :]), ALU.subtract).then_inc(lo_done, 1)
                        kt = prepared(half, g)
                        if kt is not None and not (last and half == 1):
                            split_x(unit + 1, 1 - half, kt)
                        if last:
                            continue
                        if half == 0:
                            per = NCH // (AGGREGATE_AT - STATS_AT)
                            if STATS_AT <= g < AGGREGATE_AT:
                                for c in range(per * (g - STATS_AT), per * (g - STATS_AT + 1)):
                                    chunk(b + 1, c)
                            if g == AGGREGATE_AT:
                                aggregate(b + 1)
                            if g == AGGREGATE_AT + 2:
                                deviation(b + 1)
                        elif g == 0:
                            inverse_root(b + 1)

            all_batches(dve, batch)


def attend_phase(nc, S, x, wp_dram, q_dram, k_dram, v_dram, o_dram, recip_dram, out, psum):
    B, C, N, KT, DH, MT, NH = S.B, S.C, S.N, S.KT, S.DH, S.MT, S.NH
    SLOTS = 3
    PARTS = 4
    RING = 3
    BODY = KT
    LAG = HEADS + 1
    SCALE = float(DH) ** -0.5
    SUMS_AT, OUT_AT = 1, 3
    OUT_STEPS = MT - OUT_AT
    assert BODY % SLOTS == 0 and (SLOTS * MT * 2) % RING == 0 and MT == 8 and HEADS == 2 * KT
    scores = psum[:, 0:RING, :]
    rows = psum[:, 3:5, :].rearrange("p a n -> p (a n)")
    heads = psum[:, 5:7, :].rearrange("p a n -> p (a n)")
    small = psum[:, 7, :]

    with ExitStack() as ctx:
        def sb(name, shape, dt=F32):
            return ctx.enter_context(nc.sbuf_tensor(name, shape, dt))

        def sem(name):
            return ctx.enter_context(nc.semaphore(name))

        q = sb("q", [P, SLOTS, N], F32R)
        k = sb("k", [P, SLOTS, N], F32R)
        q_m = sb("q_m", [P, SLOTS, N], F32R)
        k_m = sb("k_m", [P, SLOTS, N], F32R)
        v = sb("v", [P, SLOTS, MT, P], F32R)
        p_all = sb("p_all", [P, 2, N])
        p_hi = sb("p_hi", [P, PARTS, N], F32R)
        p_lo = sb("p_lo", [P, PARTS, N], F32R)
        sums = sb("sums", [P, SLOTS, N])
        neg_max = sb("neg_max", [P, SLOTS, MT], F32R)
        recip = sb("recip", [P, MT])
        recip_all = sb("recip_all", [DH, N])
        low_half = sb("low_half", [DH, N])
        o = sb("o", [DH, N])
        o_hi = sb("o_hi", [DH, N], F32R)
        o_lo = sb("o_lo", [DH, N], F32R)
        one = sb("one", [P, 1])
        wp = sb("wp", [P, 2, KT, C], F32R)
        a = sb("a", [P, KT, 2, BANK], F32R)
        y = sb("y", [P, 2, BANK])

        wp_in = sem("wp_in")
        qk_in = [sem(f"qk_in{s}") for s in range(SLOTS)]
        v_in = [sem(f"v_in{s}") for s in range(SLOTS)]
        set_done = sem("set_done")
        max_in = sem("max_in")
        rows_ready = sem("rows_ready")
        max_done = sem("max_done")
        s_ready = sem("s_ready")
        exp_done = sem("exp_done")
        hi_done = sem("p_hi_done")
        lo_done = sem("p_lo_done")
        added = sem("added")
        pv_done = sem("pv_done")
        sums_ready = sem("sums_ready")
        recip_done = sem("recip_done")
        recip_out = sem("recip_out")
        recip_in = sem("recip_in")
        low_done = sem("low_done")
        un_done = sem("un_done")
        o_done = sem("o_done")
        o_hi_done = sem("o_hi_done")
        o_lo_done = sem("o_lo_done")
        o_hi_out = sem("o_hi_out")
        o_lo_out = sem("o_lo_out")
        a_in = [sem(f"a_in{t}") for t in range(KT)]
        x_in = [sem(f"res_in{r}") for r in range(2)]
        group_done = sem("out_group_done")
        y_done = sem("y_done")
        y_out = [sem(f"y_out{r}") for r in range(2)]

        def known(n):
            return isinstance(n, int)

        def wait(eng, s, n):
            if not (known(n) and n <= 0):
                eng.wait_ge(s, n)

        def all_heads(eng, head):
            for g in range(LAG + BODY):
                head(g, g % BODY, g >= LAG)
            with eng.Fori(LAG // BODY + 1, (NH - 1) // BODY) as u:
                for j in range(BODY):
                    head(u * BODY + (j + 1), (j + 1) % BODY, True, u=u, j=j)
            for g in range((NH - 1) // BODY * BODY + 1, NH):
                head(g, g % BODY, True)

        assert LAG % BODY == 1 and LAG // BODY == 2

        def turn(g, ring, u, j):
            return g // ring if u is None else u * (BODY // ring) + (j + 1) // ring

        SETS = 1 + 3 * SLOTS
        block = ctx.enter_context(nc.Block())

        @block.sync
        def _(sp):
            def load(g, e, before):
                wait(sp, s_ready, before * MT * 2)
                ch = bass.ds(g * DH, DH)
                for dst, src in ((q[0:DH], q_dram[0]), (k[0:DH], k_dram[0]), (q[DH:P], q_dram[1]), (k[DH:P], k_dram[0]),
                                 (q_m[0:DH], q_dram[0]), (k_m[0:DH], k_dram[1])):
                    sp.dma_start(f32(dst[:, e, :]), src[ch, :]).then_inc(qk_in[e], 16)
                wait(sp, pv_done, before * MT)
                sp.dma_start(f32(v[:, e, :, :]), v_dram[bass.ds(g, 1)].rearrange("a p m d -> (a p) m d")).then_inc(v_in[e], 16)

            def maxima(g, e):
                sp.wait_ge(max_done, (g + 1) * MT)
                sp.dma_start(f32(q_m[DH:DH + 1, e, :]).rearrange("a (p t) -> a p t", t=MT),
                             f32(neg_max[:, e, :])).then_inc(max_in, 16)

            def head(g, m, b, hb, last=False):
                group = not (known(b) and b * HEADS + hb < LAG)
                if not (known(b) and b * HEADS + hb + 2 >= NH):
                    load(g + 2, (m + 2) % SLOTS, g)
                if group and not (known(g) and g == LAG):
                    store_group(g - LAG - 1, *where(b, hb - 1))
                if group:
                    load_group(g - LAG, *where(b, hb))
                if not (known(g) and g == 0):
                    spread(g - 1)
                if not (known(g) and g == NH - 1):
                    maxima(g + 1, (m + 1) % SLOTS)
                if not (known(g) and g == 0):
                    store_head(g - 1)

            def where(b, hb):
                n = hb - 1
                return (b - 1, n // KT, n % KT) if n >= 0 else (b - 2, 1, n + KT)

            def place(t, b, half, ot):
                return t[bass.ds(b, 1), ot * P:(ot + 1) * P, half * BANK:(half + 1) * BANK].rearrange("a p n -> (a p) n")

            def store_group(n, b, half, ot):
                sp.wait_ge(y_done, n + 1)
                sp.dma_start(place(out, b, half, ot), y[:, ot % 2, :]).then_inc(y_out[ot % 2], 16)

            def load_group(n, b, half, ot):
                if ot == 0:
                    sp.wait_ge(o_hi_out, (b + 1) * (HEADS * 16))
                    sp.wait_ge(o_lo_out, (b + 1) * (HEADS * 16))
                    for kt in range(KT):
                        sp.dma_start(f32(a[:, kt, :, :]), o_dram[:, bass.ds(b * C + kt * P, P), half * BANK:(half + 1) * BANK]
                                     .rearrange("s p n -> p s n")).then_inc(a_in[kt], 16)
                r = ot % 2
                before = b * HEADS // 2 + half * (KT // 2) + ot // 2 if known(b) else b * (HEADS // 2) + (half * (KT // 2) + ot // 2)
                wait(sp, y_out[r], 16 * before)
                sp.dma_start(y[:, r, :], place(x, b, half, ot)).then_inc(x_in[r], 16)

            def spread(g):
                sp.wait_ge(recip_done, g + 1)
                sp.dma_start(recip_dram[0], recip[:]).then_inc(recip_out, 16)
                sp.wait_ge(recip_out, 16 * (g + 1))
                sp.dma_start(recip_all[:], recip_dram[0:1].rearrange("a p t -> a (p t)").broadcast_to([DH, N])).then_inc(recip_in, 16)

            def store_head(g):
                ch = bass.ds(g * DH, DH)
                sp.wait_ge(o_hi_done, g + 1)
                sp.dma_start(o_dram[0, ch, :], f32(o_hi[:])).then_inc(o_hi_out, 16)
                sp.wait_ge(o_lo_done, g + 1)
                sp.dma_start(o_dram[1, ch, :], f32(o_lo[:])).then_inc(o_lo_out, 16)

            load(0, 0, 0)
            load(1, 1, 0)
            sp.wait_ge(set_done, SETS)
            maxima(0, 0)
            for part in range(2):
                sp.dma_start(f32(wp[:, part, :, :]), wp_dram[part].rearrange("(k p) o -> p k o", p=P)).then_inc(wp_in, 16)
            for hb in range(HEADS):
                head(hb, hb % BODY, 0, hb)
            head(HEADS, 0, 1, 0)
            for hb in range(1, HEADS):
                head(HEADS + hb, hb % BODY, 1, hb)
            with sp.Fori(2, B - 1) as b:
                for hb in range(HEADS):
                    head(b * HEADS + hb, hb % BODY, b, hb)
            for hb in range(HEADS):
                head((B - 1) * HEADS + hb, hb % BODY, B - 1, hb)
            store_group(NH - LAG - 1, *where(B - 1, HEADS - 1))
            load_group(NH - LAG, *where(B, 0))
            spread(NH - 1)
            store_head(NH - 1)
            for hb in range(1, HEADS + 1):
                store_group((B - 1) * HEADS + hb - 2, *where(B, hb - 1))
                load_group((B - 1) * HEADS + hb - 1, *where(B, hb))
            store_group(NH - 1, *where(B, HEADS))
            for r in range(2):
                sp.wait_ge(y_out[r], 16 * NH // 2)

        @block.gpsimd
        def _(pool):
            def add(g, e, t):
                if t == 1:
                    wait(pool, sums_ready, g - SLOTS + 1)
                pool.wait_ge(exp_done, (g * MT + t + 1) * 2)
                if t > 1:
                    pool.wait_ge(added, g * (MT - 1) + t - 1)
                if t == 5:
                    wait(pool, o_done, g)
                if t == 7:
                    wait(pool, o_lo_done, g)
                first = p_all[:, 0, :] if t == 1 else sums[:, e, :]
                pool.tensor_tensor(sums[:, e, :], first, p_all[:, t % 2, :], ALU.add).then_inc(added, 1)

            def divide(g, adds):
                pool.wait_ge(added, adds)
                pool.wait_ge(recip_in, 16 * (g + 1))
                pool.wait_ge(un_done, g + 1)
                pool.tensor_tensor(o[:], o[:], recip_all[:], ALU.mult).then_inc(o_done, 1)

            def low_out(g, adds):
                pool.wait_ge(added, adds)
                pool.wait_ge(o_hi_done, g + 1)
                wait(pool, o_lo_out, 16 * g)
                pool.tensor_tensor(o_lo[:], o[:], f32(o_hi[:]), ALU.subtract).then_inc(o_lo_done, 1)

            def head(g, m, groups, u=None, j=None):
                for t in range(MT):
                    if t:
                        add(g, m % SLOTS, t)
                    if not (known(g) and g == 0):
                        if t == 4:
                            divide(g - 1, g * (MT - 1) + 4)
                        elif t == 6:
                            low_out(g - 1, g * (MT - 1) + 6)

            all_heads(pool, head)
            divide(NH - 1, NH * (MT - 1))
            low_out(NH - 1, NH * (MT - 1))

        @block.tensor
        def _(pe):
            PRODUCTS = [(kt, wpart, apart) for kt in range(KT) for wpart, apart in ((0, 0), (0, 1), (1, 0))]
            PER_STEP = -(-len(PRODUCTS) // OUT_STEPS)

            def scores_by_query(g, e, t, count):
                if count is not None:
                    pe.wait_ge(qk_in[e], 96 * count)
                wait(pe, max_done, g * MT + t)
                queries = q[:, e, :].rearrange("p (n t) -> p t n", t=MT)[:, t, :]
                for h in range(2):
                    mm = pe.matmul(rows[:, h * BANK:(h + 1) * BANK], queries, k[:, e, h * BANK:(h + 1) * BANK],
                                   start=True, stop=True)
                mm.then_inc(rows_ready, 1)

            def scores_by_key(g, e, t):
                if t == 0:
                    pe.wait_ge(max_in, 16 * (g + 1))
                for h in range(2):
                    n = (g * MT + t) * 2 + h
                    r = ((e * MT + t) * 2 + h) % RING
                    cols, keys = slice(h * BANK, (h + 1) * BANK), slice(t * P, (t + 1) * P)
                    wait(pe, exp_done, n - RING + 1)
                    pe.matmul(scores[:, r, :], k[:, e, keys], q[:, e, cols], start=True, stop=False)
                    pe.matmul(scores[:, r, :], k_m[:, e, keys], q_m[:, e, cols], start=False,
                              stop=True).then_inc(s_ready, 1)

            def values(g, e, t, count=None):
                pe.wait_ge(lo_done, g * MT + t + 1)
                if t == 0:
                    wait(pe, un_done, g)
                    pe.wait_ge(v_in[e], 16 * count)
                r = t % PARTS
                for h in range(2):
                    cols = slice(h * BANK, (h + 1) * BANK)
                    pe.matmul(heads[:, cols], v[:, e, t, :], p_hi[:, r, cols], start=(t == 0), stop=False)
                    mm = pe.matmul(heads[:, cols], v[:, e, t, :], p_lo[:, r, cols], start=False, stop=(t == MT - 1))
                mm.then_inc(pv_done, 1)

            def add_up(g, e):
                pe.wait_ge(added, (g + 1) * (MT - 1))
                wait(pe, y_done, g - LAG + 1)
                for t in range(MT):
                    queries = sums[:, e, :].rearrange("p (n t) -> p t n", t=MT)[:, t, :]
                    mm = pe.matmul(small[:, t:t + 1], queries, one[:, 0:1], start=True, stop=True)
                mm.then_inc(sums_ready, 1)

            def output(bank, ot, products, count):
                for kt, wpart, apart in products:
                    first = (kt, wpart, apart) == PRODUCTS[0]
                    final = (kt, wpart, apart) == PRODUCTS[-1]
                    if ot == 0 and (wpart, apart) == (0, 0):
                        pe.wait_ge(a_in[kt], 16 * count)
                    mm = pe.matmul(bank, wp[:, wpart, kt, ot * P:(ot + 1) * P], a[:, kt, apart, :], start=first, stop=final)
                    if final:
                        mm.then_inc(group_done, 1)

            pe.wait_ge(set_done, SETS)
            for t in range(MT):
                scores_by_query(0, 0, t, 1 if t == 0 else None)

            def head(g, m, groups, u=None, j=None):
                e, nxt, prev = m % SLOTS, (m + 1) % SLOTS, (m - 1) % SLOTS
                first, last = known(g) and g == 0, known(g) and g == NH - 1
                for t in range(MT):
                    scores_by_key(g, e, t)
                    if not last and t < MT - 1:
                        for n in ((t,) if t < 3 else (3, 4) if t == 3 else (t + 1,)):
                            count = None
                            if n == 0:
                                count = (g + 1) // SLOTS + 1 if u is None else u * (BODY // SLOTS) + ((j + 2) // SLOTS + 1)
                            scores_by_query(g + 1, nxt, n, count)
                    if t == 0 and not first:
                        values(g - 1, prev, MT - 1)
                    if t == 2:
                        values(g, e, 0, turn(g, SLOTS, u, j) + 1)
                        values(g, e, 1)
                    elif t > 2:
                        values(g, e, t - 1)
                    if t == SUMS_AT and not first:
                        add_up(g - 1, prev)
                    if groups and t >= OUT_AT:
                        if t == OUT_AT:
                            pe.wait_ge(recip_done, g)
                            if known(g) and g == LAG or u is not None and j == 0:
                                pe.wait_ge(wp_in, 32)
                        ot = (m - 1) % BODY
                        i = (t - OUT_AT) * PER_STEP
                        count = None if ot else (g - LAG) // KT + 1 if u is None else u - 1
                        output(small, ot, PRODUCTS[i:i + PER_STEP], count)

            all_heads(pe, head)
            values(NH - 1, (NH - 1) % SLOTS, MT - 1)
            add_up(NH - 1, (NH - 1) % SLOTS)
            pe.wait_ge(recip_done, NH)
            for n in range(NH - LAG, NH):
                wait(pe, y_done, n - 1 if n > NH - LAG else n)
                output(psum[:, 7 if n % 2 else 0, :], n % KT, PRODUCTS, n // KT + 1)

        @block.scalar
        def _(act):
            def take_low(g):
                act.wait_ge(pv_done, (g + 1) * MT)
                wait(act, un_done, g)
                act.copy(low_half[:], heads[DH:P, :]).then_inc(low_done, 1)

            def high_out(g):
                act.wait_ge(o_done, g + 1)
                wait(act, o_hi_out, 16 * g)
                act.copy(o_hi[:], o[:]).then_inc(o_hi_done, 1)

            def head(g, m, groups, u=None, j=None):
                begins = known(g) and g == 0
                for t in range(MT):
                    n = g * MT + t
                    if t == 1 and not begins:
                        take_low(g - 1)
                    wait(act, added, g * (MT - 1) + (t - 2 if t > 2 else t - 1))
                    wait(act, lo_done, n - 1)
                    for h in range(2):
                        r = ((m % SLOTS * MT + t) * 2 + h) % RING
                        act.wait_ge(s_ready, 2 * n + h + 1)
                        act.activation(p_all[:, t % 2, h * BANK:(h + 1) * BANK], scores[:, r, :], ACT.Exp,
                                       scale=SCALE).then_inc(exp_done, 1)
                    act.wait_ge(exp_done, 2 * n + 2)
                    wait(act, pv_done, n - PARTS + 1)
                    act.copy(p_hi[:, t % PARTS, :], p_all[:, t % 2, :]).then_inc(hi_done, 1)
                    if not begins:
                        if t == 5:
                            high_out(g - 1)

            all_heads(act, head)
            take_low(NH - 1)
            high_out(NH - 1)

        @block.vector
        def _(dve):
            def row_max(g, e, t):
                dve.wait_ge(rows_ready, g * MT + t + 1)
                if t == 0:
                    wait(dve, max_in, 16 * (g - SLOTS + 1))
                dve.tensor_reduce(neg_max[:, e, t:t + 1], rows, AX.X, ALU.max, negate=True).then_inc(max_done, 1)

            def low_part(g, t):
                n = g * MT + t
                dve.wait_ge(hi_done, n + 1)
                dve.tensor_tensor(p_lo[:, t % PARTS, :], p_all[:, t % 2, :], f32(p_hi[:, t % PARTS, :]),
                                  ALU.subtract).then_inc(lo_done, 1)

            def take_head(g):
                dve.wait_ge(low_done, g + 1)
                wait(dve, o_hi_done, g)
                wait(dve, o_lo_done, g)
                dve.tensor_tensor(o[:], heads[0:DH, :], low_half[:], ALU.add).then_inc(un_done, 1)

            def reciprocals(g):
                dve.wait_ge(sums_ready, g + 1)
                wait(dve, recip_out, 16 * g)
                dve.reciprocal(recip[:], small[:, 0:MT]).then_inc(recip_done, 1)

            def add_x(n, r, count, bank=small):
                dve.wait_ge(group_done, n + 1)
                dve.wait_ge(x_in[r], 16 * count)
                dve.tensor_tensor(y[:, r, :], bank, y[:, r, :], ALU.add).then_inc(y_done, 1)

            dve.memset(one[:], 1.0).then_inc(set_done, 1)
            for e in range(SLOTS):
                dve.memset(f32(q_m[DH:P, e, :]), 0.0).then_inc(set_done, 1)
                dve.memset(f32(k_m[DH:P, e, :]), 0.0).then_inc(set_done, 1)
            dve.wait_ge(set_done, 1 + 2 * SLOTS)
            for e in range(SLOTS):
                dve.memset(f32(k_m[DH:DH + 1, e, :]), 1.0).then_inc(set_done, 1)

            for t in range(MT):
                row_max(0, 0, t)

            def head(g, m, groups, u=None, j=None):
                begins, last = known(g) and g == 0, known(g) and g == NH - 1
                nxt = (m + 1) % SLOTS
                for t in range(MT):
                    if t == SUMS_AT + 1 and not begins:
                        reciprocals(g - 1)
                    if not last and t < MT - 1:
                        for n in ((t,) if t < 3 else (3, 4) if t == 3 else (t + 1,)):
                            row_max(g + 1, nxt, n)
                    if t == 1 and not begins:
                        take_head(g - 1)
                    low_part(g, t)
                    if t == 0 and not (known(g) and g <= LAG):
                        n, r = g - LAG - 1, m % 2
                        add_x_when(n, r, g, u, j)

            def add_x_when(n, r, g, u, j):
                if u is not None:
                    add_x(n, r, u * (BODY // 2) + ((j - LAG) // 2 + 1))
                else:
                    add_x(n, r, n // 2 + 1)

            all_heads(dve, head)
            take_head(NH - 1)
            add_x(NH - LAG - 1, (NH - LAG - 1) % 2, (NH - LAG - 1) // 2 + 1)
            reciprocals(NH - 1)
            for n in range(NH - LAG, NH):
                add_x(n, n % 2, n // 2 + 1, psum[:, 7 if n % 2 else 0, :])


def build(nc, x, wq, wk, wv, wp, ident_in, avg_in, scratch, out):
    S = Shapes(x)
    assert S.C % P == 0 and S.N == 2 * BANK and 2 * S.DH == P and (S.C // GROUPS) % S.KT == 0
    q_dram, k_dram, v_dram, o_dram, wp_dram, recip_dram = scratch
    with nc.psum_tensor("psum", [P, 8, BANK], F32) as psum:
        project_phase(nc, S, x, (wp, wq, wk, wv), ident_in, avg_in, wp_dram, q_dram, k_dram, v_dram, psum)
        attend_phase(nc, S, x, wp_dram, q_dram, k_dram, v_dram, o_dram, recip_dram, out, psum)


def kernel(x, L0_conv_Wq, L0_conv_Wk, L0_conv_Wv, L0_conv_Wp):
    import numpy as np
    import concourse.bacc as bacc
    from concourse.bass_utils import run_bass_kernel_spmd

    nc = bacc.Bacc("TRN2", target_bir_lowering=False, num_devices=1)
    Bn, Cn, Hn, Wn = x.shape
    Nn, Dn = Hn * Wn, Cn // HEADS
    per_group = Cn // GROUPS // (Cn // P)
    arrays = {
        "x": np.ascontiguousarray(x).reshape(Bn, Cn, Nn),
        "wq": np.ascontiguousarray(L0_conv_Wq), "wk": np.ascontiguousarray(L0_conv_Wk),
        "wv": np.ascontiguousarray(L0_conv_Wv), "wp": np.ascontiguousarray(L0_conv_Wp),
        "ident": np.eye(P, dtype=np.float32),
        "avg": np.kron(np.eye(P // per_group), np.full((per_group, per_group), 1.0 / per_group)).astype(np.float32),
    }
    args = [nc.dram_tensor("in_" + n, a.shape, F32, kind="ExternalInput").ap() for n, a in arrays.items()]
    shapes = {
        "q_parts": (2, Bn * Cn, Nn), "k_parts": (2, Bn * Cn, Nn), "v_parts": (Bn * HEADS, P, Nn // P, 2 * Dn),
        "o_parts": (2, Bn * Cn, Nn), "wp_parts": (2, Cn, Cn), "recip_rows": (2, P, Nn // P),
    }
    scratch = [nc.dram_tensor(n, s, F32, kind="Internal").ap() for n, s in shapes.items()]
    out = nc.dram_tensor("out", (Bn, Cn, Nn), F32, kind="ExternalOutput").ap()
    build(nc, *args, scratch, out)
    got = run_bass_kernel_spmd(nc, [{"in_" + n: a for n, a in arrays.items()}], core_ids=[0])
    return got.results[0]["out"].reshape(Bn, Cn, Hn, Wn)
```

```python
from contextlib import ExitStack

import concourse.bass as bass
from concourse import mybir

F32 = mybir.dt.float32
F32R = mybir.dt.float32r
I32 = mybir.dt.int32
ALU = mybir.AluOpType
ACT = mybir.ActivationFunctionType
AX = mybir.AxisListType

P = 128
BANK = 512
HEADS = 12
GROUPS = 32
EPS = 1e-5


def f32(ap):
    return ap.bitcast(F32)


class Shapes:
    def __init__(self, x):
        self.B, self.C, self.N = x.shape
        self.KT = self.C // P
        self.DH = self.C // HEADS
        self.HALVES = self.N // BANK
        self.MT = self.N // P
        self.NH = self.B * HEADS


def project_phase(nc, S, x, weights, ident_in, avg_in, wp_dram, q_dram, k_dram, v_dram, psum):
    B, C, N, KT, DH = S.B, S.C, S.N, S.KT, S.DH
    TP = 3
    WG = KT * KT // TP
    VC = C // 2
    VH = VC // DH
    NT = BANK // P
    RING = 4
    PER_HALF = 2 * KT + 2 * NT
    NCH = C * N // P // BANK
    assert PER_HALF % RING == 0

    with ExitStack() as ctx:
        def sb(name, shape, dt=F32):
            return ctx.enter_context(nc.sbuf_tensor(name, shape, dt))

        def sem(name):
            return ctx.enter_context(nc.semaphore(name))

        w_hi = sb("w_hi", [P, 3, KT, C], F32R)
        w_lo = sb("w_lo", [P, 3, KT, C], F32R)
        x_raw = sb("x_raw", [P, KT, N])
        w_nat = x_raw[:, :, 0:C]
        xn = sb("xn", [P, 2, BANK])
        xn_hi = sb("xn_hi", [P, 2, KT, BANK], F32R)
        xn_lo = sb("xn_lo", [P, 2, KT, BANK], F32R)
        stage = sb("stage", [P, RING, 2 * BANK], F32R)
        ident = sb("ident_a", [P, P])
        wp_hi = xn_hi[:, :, :, :].rearrange("p a k n -> p (a k n)")[:, 0:KT * C].rearrange("p (k o) -> p k o", k=KT)
        wp_lo = xn_lo[:, :, :, :].rearrange("p a k n -> p (a k n)")[:, 0:KT * C].rearrange("p (k o) -> p k o", k=KT)
        avg = sb("avg", [P, P])
        stats = sb("stats", [P, NCH, 6])
        mom = sb("mom", [P, 2])
        mean = sb("mean", [P, 1])
        dev = sb("dev", [P, 1])
        spread = sb("spread", [P, 1])
        var = sb("var", [P, 1])
        yi = sb("yi", [P, 1], I32)
        yf = sb("yf", [P, 1])
        rs = sb("rs", [P, 1])
        t0 = sb("t0", [P, 1])
        t1 = sb("t1", [P, 1])
        shift = sb("shift", [P, 1])

        const_in = sem("const_in")
        w_in = sem("w_in")
        w_turned = sem("w_turned")
        w_hi_done = sem("w_hi_done")
        w_lo_done = sem("w_lo_done")
        wp_out = sem("wp_out")
        x_in = sem("x_in")
        stats_step = sem("stats_step")
        bn_done = sem("bn_done")
        mean_ps = sem("mean_ps")
        dev_done = sem("dev_done")
        var_ps = sem("var_ps")
        norm_done = sem("norm_done")
        xn_made = sem("xn_made")
        xn_hi_done = sem("xn_hi_done")
        xn_lo_done = sem("xn_lo_done")
        group_done = sem("group_done")
        hi_done = sem("hi_done")
        lo_done = sem("lo_done")
        stored = [sem(f"stored{r}") for r in range(RING)]

        x_v = x.rearrange("b (p k) n -> b p k n", k=KT)

        CHAIN = 5 + 3 * 4 + 1
        NEXT_AT = (0, 2)
        STATS_AT, AGGREGATE_AT = 11, 17

        def known(n):
            return isinstance(n, int)

        def wait(eng, s, n):
            if not (known(n) and n <= 0):
                eng.wait_ge(s, n)

        STORES = [sum(2 if g < 2 * KT else 1 for g in range(r, PER_HALF, RING)) for r in range(RING)]

        def stored_before(unit, g):
            r = g % RING
            return 16 * (unit * STORES[r] + sum(2 if h < 2 * KT else 1 for h in range(r, g, RING)))

        def all_batches(eng, batch):
            batch(0, False)
            with eng.Fori(1, B - 1) as b:
                batch(b, False)
            batch(B - 1, True)

        def prepared(half, g):
            kt = g - NEXT_AT[half]
            return kt if 0 <= kt < KT else None

        block = ctx.enter_context(nc.Block())

        @block.sync
        def _(sp):
            sp.dma_start(ident[:], ident_in).then_inc(const_in, 16)
            sp.dma_start(avg[:], avg_in).then_inc(const_in, 16)
            for w in range(4):
                if w >= 1:
                    sp.wait_ge(w_turned, w * WG)
                sp.dma_start(w_nat, weights[w].rearrange("(o p) c -> p o c", p=P)).then_inc(w_in, 16)
                if w == 1:
                    sp.wait_ge(w_lo_done, WG)
                    for part, src in enumerate((wp_hi, wp_lo)):
                        sp.dma_start(wp_dram[part].rearrange("(k p) o -> p k o", p=P), f32(src)).then_inc(wp_out, 16)
            sp.wait_ge(w_turned, 4 * WG)
            sp.dma_start(x_raw[:], x_v[0]).then_inc(x_in, 16)

            def batch(b, last):
                for half in range(S.HALVES):
                    for g in range(PER_HALF):
                        r = g % RING
                        if half == 0 and g == NEXT_AT[0] + KT and not last:
                            sp.wait_ge(xn_made, (b + 1) * S.HALVES * KT)
                            sp.dma_start(x_raw[:], x_v[bass.ds(b + 1, 1)]).then_inc(x_in, 16)
                        sp.wait_ge(lo_done, (b * S.HALVES + half) * PER_HALF + g + 1)
                        if g < 2 * KT:
                            dst = q_dram if g < KT else k_dram
                            rows = bass.ds(b * C + g % KT * P, P)
                            for part in range(2):
                                sp.dma_start(dst[part, rows, half * BANK:(half + 1) * BANK],
                                             f32(stage[:, r, part * BANK:(part + 1) * BANK])).then_inc(stored[r], 16)
                        else:
                            nt, cg = (g - 2 * KT) // 2, (g - 2 * KT) % 2
                            sp.dma_start(v_dram[bass.ds(b * HEADS + cg * VH, VH), :, half * NT + nt, :].rearrange("h p d -> p h d"),
                                         f32(stage[:, r, 0:2 * VC]).rearrange("p (h d) -> p h d", h=VH)).then_inc(stored[r], 16)

            all_batches(sp, batch)
            sp.wait_ge(wp_out, 32)
            for r in range(RING):
                sp.wait_ge(stored[r], 16 * STORES[r] * S.HALVES * B)

        @block.tensor
        def _(pe):
            pe.wait_ge(const_in, 32)
            for w in range(4):
                pe.wait_ge(w_in, 16 * (w + 1))
                for g in range(WG):
                    n = w * WG + g
                    wait(pe, w_lo_done, n - RING + 1)
                    kt, o0 = g // (KT // TP), g % (KT // TP) * TP
                    src = w_nat.rearrange("p o (k c) -> p o k c", k=KT) if w == 0 else \
                        w_nat.rearrange("p o (c k) -> p o k c", k=KT)
                    for o in range(TP):
                        mm = pe.transpose(psum[:, n % RING, o * P:(o + 1) * P], src[:, o0 + o, kt, :], ident[:])
                    mm.then_inc(w_turned, 1)

            def mean_product(b):
                pe.wait_ge(stats_step, CHAIN * b + 1)
                pe.matmul(psum[:, RING, 0:1], avg[:], mom[:, 0:1], start=True, stop=True).then_inc(mean_ps, 1)

            def variance_product(b):
                pe.wait_ge(dev_done, b + 1)
                pe.matmul(psum[:, RING + 1, 0:1], avg[:], spread[:], start=True, stop=True).then_inc(var_ps, 1)

            def project(b, half, last):
                unit = b * S.HALVES + half
                for g in range(PER_HALF):
                    r = g % RING
                    wait(pe, lo_done, unit * PER_HALF + g - RING + 1)
                    out = psum[:, r, :]
                    for kt in range(KT):
                        if g == 0:
                            pe.wait_ge(xn_lo_done, unit * KT + kt + 1)
                        a, z = xn_hi[:, half, kt, :], xn_lo[:, half, kt, :]
                        if g < 2 * KT:
                            w, cols = g // KT, slice(g % KT * P, (g % KT + 1) * P)
                            wa, wz = w_hi[:, w, kt, cols], w_lo[:, w, kt, cols]
                            parts = [(wa, a), (wa, z), (wz, a)]
                        else:
                            nt, cg = (g - 2 * KT) // 2, (g - 2 * KT) % 2
                            t, cols = slice(nt * P, (nt + 1) * P), slice(cg * VC, (cg + 1) * VC)
                            va, vz = w_hi[:, 2, kt, cols], w_lo[:, 2, kt, cols]
                            parts = [(a[:, t], va), (a[:, t], vz), (z[:, t], va)]
                            out = psum[:, r, 0:VC]
                        for n, (lhs, rhs) in enumerate(parts):
                            mm = pe.matmul(out, lhs, rhs, start=(kt == 0 and n == 0), stop=(kt == KT - 1 and n == 2))
                    mm.then_inc(group_done, 1)
                    if half == 0 and not last:
                        if g == AGGREGATE_AT + 1:
                            mean_product(b + 1)
                        if g == AGGREGATE_AT + 2:
                            variance_product(b + 1)

            mean_product(0)
            variance_product(0)

            def batch(b, last):
                project(b, 0, last)
                project(b, 1, last)

            all_batches(pe, batch)

        @block.scalar
        def _(act):
            for n in range(4 * WG):
                w, g = n // WG, n % WG
                kt, o0 = g // (KT // TP), g % (KT // TP) * TP
                cols = slice(o0 * P, (o0 + TP) * P)
                act.wait_ge(w_turned, n + 1)
                act.copy((wp_hi if w == 0 else w_hi[:, w - 1])[:, kt, cols], psum[:, n % RING, 0:TP * P]).then_inc(w_hi_done, 1)

            def normalise(unit, half, kt):
                wait(act, xn_lo_done, unit * KT + kt - 1)
                act.activation(xn[:, kt % 2, :], x_raw[:, kt, half * BANK:(half + 1) * BANK], ACT.Identity,
                               bias=shift[:, 0:1], scale=rs[:, 0:1]).then_inc(xn_made, 1)

            act.wait_ge(norm_done, 1)
            for kt in range(KT):
                normalise(0, 0, kt)

            def batch(b, last):
                for half in range(S.HALVES):
                    unit = b * S.HALVES + half
                    for g in range(PER_HALF):
                        r = g % RING
                        act.wait_ge(group_done, unit * PER_HALF + g + 1)
                        wait(act, stored[r], stored_before(unit, g))
                        if g < 2 * KT:
                            dst, src = stage[:, r, 0:BANK], psum[:, r, :]
                        else:
                            dst = stage[:, r, 0:2 * VC].rearrange("p (h s d) -> p h s d", h=VH, s=2)[:, :, 0, :]
                            src = psum[:, r, 0:VC].rearrange("p (h d) -> p h d", h=VH)
                        act.copy(dst, src).then_inc(hi_done, 1)
                        kt = prepared(half, g)
                        if kt is not None and not (last and half == 1):
                            if half == 1 and kt == 0:
                                act.wait_ge(norm_done, b + 2)
                            normalise(unit + 1, 1 - half, kt)

            all_batches(act, batch)

        @block.vector
        def _(dve):
            for n in range(4 * WG):
                w, g = n // WG, n % WG
                kt, o0 = g // (KT // TP), g % (KT // TP) * TP
                cols = slice(o0 * P, (o0 + TP) * P)
                hi, lo = (wp_hi, wp_lo) if w == 0 else (w_hi[:, w - 1], w_lo[:, w - 1])
                dve.wait_ge(w_hi_done, n + 1)
                dve.tensor_tensor(lo[:, kt, cols], psum[:, n % RING, 0:TP * P], f32(hi[:, kt, cols]),
                                  ALU.subtract).then_inc(w_lo_done, 1)

            def link(op, b, n):
                op.then_inc(stats_step, 1)
                dve.wait_ge(stats_step, CHAIN * b + n)

            def chunk(b, c):
                if c == 0:
                    dve.wait_ge(x_in, 16 * (b + 1))
                kt, h = c // S.HALVES, c % S.HALVES
                op = dve.bn_stats(stats[:, c, :], x_raw[:, kt, h * BANK:(h + 1) * BANK])
                if c == NCH - 1:
                    op.then_inc(bn_done, 1)

            def aggregate(b):
                dve.wait_ge(bn_done, b + 1)
                dve.tensor_copy(t0[:], stats[:, 0, 0:1])
                dve.bn_aggr(mom[:], stats[:]).then_inc(stats_step, 1)

            def deviation(b):
                dve.wait_ge(mean_ps, b + 1)
                link(dve.tensor_copy(mean[:], psum[:, RING, 0:1]), b, 2)
                link(dve.tensor_tensor(dev[:], mom[:, 0:1], mean[:], ALU.subtract), b, 3)
                dve.scalar_tensor_tensor(spread[:], dev[:], dev[:, 0:1], mom[:, 1:2], ALU.mult, ALU.add).then_inc(dev_done, 1)

            def inverse_root(b):
                dve.wait_ge(var_ps, b + 1)
                link(dve.tensor_scalar(var[:], psum[:, RING + 1, 0:1], EPS, None, ALU.add), b, 4)
                link(dve.tensor_scalar(yi[:], var[:].bitcast(I32), 1, None, ALU.arith_shift_right), b, 5)
                wait(dve, xn_made, b * S.HALVES * KT)
                link(dve.tensor_scalar(rs[:].bitcast(I32), yi[:], -1.0, float(0x5F3759DF), ALU.mult, ALU.add), b, 6)
                for n in range(4):
                    link(dve.scalar_tensor_tensor(t0[:], rs[:], rs[:, 0:1], var[:], ALU.mult, ALU.mult), b, 7 + 3 * n)
                    link(dve.tensor_scalar(t1[:], t0[:], -0.5, 1.5, ALU.mult, ALU.add), b, 8 + 3 * n)
                    link(dve.tensor_tensor(rs[:], rs[:], t1[:], ALU.mult), b, 9 + 3 * n)
                dve.scalar_tensor_tensor(shift[:], mean[:], -1.0, rs[:], ALU.mult, ALU.mult).then_inc(norm_done, 1)

            def split_x(unit, half, kt):
                n = unit * KT + kt + 1
                if kt == 0:
                    wait(dve, group_done, (unit - 1) * PER_HALF)
                dve.wait_ge(xn_made, n)
                dve.tensor_copy(xn_hi[:, half, kt, :], xn[:, kt % 2, :]).then_inc(xn_hi_done, 1)
                dve.wait_ge(xn_hi_done, n)
                dve.tensor_tensor(xn_lo[:, half, kt, :], xn[:, kt % 2, :], f32(xn_hi[:, half, kt, :]),
                                  ALU.subtract).then_inc(xn_lo_done, 1)

            for c in range(NCH):
                chunk(0, c)
            aggregate(0)
            deviation(0)
            inverse_root(0)
            dve.wait_ge(wp_out, 32)
            for kt in range(KT):
                split_x(0, 0, kt)

            def batch(b, last):
                for half in range(S.HALVES):
                    unit = b * S.HALVES + half
                    for g in range(PER_HALF):
                        r = g % RING
                        dve.wait_ge(hi_done, unit * PER_HALF + g + 1)
                        if g < 2 * KT:
                            dve.tensor_tensor(stage[:, r, BANK:2 * BANK], psum[:, r, :], f32(stage[:, r, 0:BANK]),
                                              ALU.subtract).then_inc(lo_done, 1)
                        else:
                            both = stage[:, r, 0:2 * VC].rearrange("p (h s d) -> p h s d", h=VH, s=2)
                            dve.tensor_tensor(both[:, :, 1, :], psum[:, r, 0:VC].rearrange("p (h d) -> p h d", h=VH),
                                              f32(both[:, :, 0, :]), ALU.subtract).then_inc(lo_done, 1)
                        kt = prepared(half, g)
                        if kt is not None and not (last and half == 1):
                            split_x(unit + 1, 1 - half, kt)
                        if last:
                            continue
                        if half == 0:
                            per = NCH // (AGGREGATE_AT - STATS_AT)
                            if STATS_AT <= g < AGGREGATE_AT:
                                for c in range(per * (g - STATS_AT), per * (g - STATS_AT + 1)):
                                    chunk(b + 1, c)
                            if g == AGGREGATE_AT:
                                aggregate(b + 1)
                            if g == AGGREGATE_AT + 2:
                                deviation(b + 1)
                        elif g == 0:
                            inverse_root(b + 1)

            all_batches(dve, batch)


def attend_phase(nc, S, x, wp_dram, q_dram, k_dram, v_dram, o_dram, recip_dram, out, psum):
    B, C, N, KT, DH, MT, NH = S.B, S.C, S.N, S.KT, S.DH, S.MT, S.NH
    SLOTS = 3
    PARTS = 4
    RING = 3
    BODY = KT
    EXPS = 3
    LAG = HEADS + 3
    SCALE = float(DH) ** -0.5
    OUT_BY_STEP = (2, 2, 7, 0, 2, 2, 1, 2)
    EARLY = 4
    assert sum(OUT_BY_STEP) == 3 * KT and (SLOTS * MT) % EXPS == 0
    assert BODY % SLOTS == 0 and (SLOTS * MT * 2) % RING == 0 and MT == 8 and HEADS == 2 * KT
    scores = psum[:, 0:RING, :]
    rows = psum[:, 3:5, :].rearrange("p a n -> p (a n)")
    heads = psum[:, 5:7, :].rearrange("p a n -> p (a n)")
    small = psum[:, 7, :]

    with ExitStack() as ctx:
        def sb(name, shape, dt=F32):
            return ctx.enter_context(nc.sbuf_tensor(name, shape, dt))

        def sem(name):
            return ctx.enter_context(nc.semaphore(name))

        q = sb("q", [P, SLOTS, N], F32R)
        k = sb("k", [P, SLOTS, N], F32R)
        q_m = sb("q_m", [P, SLOTS, N], F32R)
        k_m = sb("k_m", [P, SLOTS, N], F32R)
        v = sb("v", [P, SLOTS, MT, P], F32R)
        p_all = sb("p_all", [P, EXPS, N])
        p_hi = sb("p_hi", [P, PARTS, N], F32R)
        p_lo = sb("p_lo", [P, PARTS, N], F32R)
        sums = sb("sums", [P, SLOTS, N])
        neg_max = sb("neg_max", [P, SLOTS, MT], F32R)
        recip = sb("recip", [P, MT])
        recip_all = sb("recip_all", [DH, N])
        o = sb("o", [DH, 2, N])
        o_hi = sb("o_hi", [DH, N], F32R)
        o_lo = sb("o_lo", [DH, N], F32R)
        one = sb("one", [P, 1])
        wp = sb("wp", [P, 2, KT, C], F32R)
        a = sb("a", [P, KT, 2, BANK], F32R)
        y = sb("y", [P, 2, BANK])
        a_of = [a[:, kt, :, :] for kt in range(KT)]
        a_last = [(q, k)[kt // SLOTS][:, kt % SLOTS, :].rearrange("p (s n) -> p s n", s=2) for kt in range(KT)]

        wp_in = sem("wp_in")
        qk_in = [sem(f"qk_in{s}") for s in range(SLOTS)]
        v_in = [sem(f"v_in{s}") for s in range(SLOTS)]
        set_done = sem("set_done")
        max_in = sem("max_in")
        rows_ready = sem("rows_ready")
        max_done = sem("max_done")
        s_ready = sem("s_ready")
        exp_done = sem("exp_done")
        hi_done = sem("p_hi_done")
        lo_done = sem("p_lo_done")
        added = sem("added")
        pv_done = sem("pv_done")
        sums_ready = sem("sums_ready")
        recip_done = sem("recip_done")
        recip_out = sem("recip_out")
        recip_in = sem("recip_in")
        low_done = sem("low_done")
        un_done = sem("un_done")
        o_done = sem("o_done")
        o_hi_done = sem("o_hi_done")
        o_lo_done = sem("o_lo_done")
        o_out = sem("o_out")
        a_in = [sem(f"a_in{t}") for t in range(KT)]
        a_last_in = [sem(f"a_last_in{t}") for t in range(KT)]
        x_in = [sem(f"res_in{r}") for r in range(2)]
        kt_done = sem("out_kt_done")
        y_done = sem("y_done")
        y_out = [sem(f"y_out{r}") for r in range(2)]

        def known(n):
            return isinstance(n, int)

        def wait(eng, s, n):
            if not (known(n) and n <= 0):
                eng.wait_ge(s, n)

        def all_heads(eng, head):
            for g in range(PEELED):
                head(g, g % BODY, g >= LAG)
            with eng.Fori(PEELED // BODY, NH // BODY - 1) as u:
                for j in range(BODY):
                    head(u * BODY + j, j, True, u=u)
            for g in range(NH - BODY, NH):
                head(g, g % BODY, True)

        PEELED = (LAG // BODY + 1) * BODY
        assert NH % BODY == 0 and PEELED >= LAG + 3

        def turn(g, ring, u, m):
            return g // ring if u is None else u * (BODY // ring) + m // ring

        def exps(e, t):
            return (e * MT + t) % EXPS

        DIVIDE_AT, HIGH_AT = 2, 6
        SETS = 1 + 3 * SLOTS
        block = ctx.enter_context(nc.Block())

        @block.sync
        def _(sp):
            def load(g, e, before, stored=None):
                wait(sp, s_ready, before * MT * 2)
                ch = bass.ds(g * DH, DH)
                for dst, src in ((q[0:DH], q_dram[0]), (k[0:DH], k_dram[0]), (q[DH:P], q_dram[1]), (k[DH:P], k_dram[0]),
                                 (q_m[0:DH], q_dram[0])):
                    sp.dma_start(f32(dst[:, e, :]), src[ch, :]).then_inc(qk_in[e], 16)
                if stored is not None:
                    sp.wait_ge(o_out, stored)
                sp.dma_start(f32(k_m[0:DH, e, :]), k_dram[1, ch, :]).then_inc(qk_in[e], 16)
                wait(sp, pv_done, before * MT)
                sp.dma_start(f32(v[:, e, :, :]), v_dram[bass.ds(g, 1)].rearrange("a p m d -> (a p) m d")).then_inc(v_in[e], 16)

            def maxima(g, e):
                sp.wait_ge(max_done, (g + 1) * MT)
                sp.dma_start(f32(q_m[DH:DH + 1, e, :]).rearrange("a (p t) -> a p t", t=MT),
                             f32(neg_max[:, e, :])).then_inc(max_in, 16)

            def head(g, m, b, hb):
                number = b * HEADS + hb if known(b) else None
                if number is None or number >= 2:
                    spread(g - 2)
                if number is None or number > LAG:
                    store_group(g - LAG - 1, *where(b, hb - 1))
                if number is None or number >= LAG:
                    load_x(*where(b, hb))
                if number is None or number >= 3:
                    store_head(g - 3)
                begins = (hb + 1 - LAG) % KT == 0 and (number is None or number + 1 >= LAG)
                if number is None or number + 2 < NH:
                    load(g + 2, (m + 2) % SLOTS, g, (where(b, hb + 1)[0] + 1) * (HEADS * 32) if begins else None)
                if begins:
                    for kt in range(EARLY):
                        load_a(g - LAG, *where(b, hb + 1)[:2], kt)
                if number is None or number < NH - 1:
                    maxima(g + 1, (m + 1) % SLOTS)
                if begins:
                    for kt in range(EARLY, KT):
                        load_a(g - LAG, *where(b, hb + 1)[:2], kt)

            def where(b, hb):
                n = hb - (LAG - HEADS)
                return (b - 1, n // KT, n % KT) if n >= 0 else (b - 2, 1, n + KT)

            def place(t, b, half, ot):
                return t[bass.ds(b, 1), ot * P:(ot + 1) * P, half * BANK:(half + 1) * BANK].rearrange("a p n -> (a p) n")

            def store_group(n, b, half, ot):
                sp.wait_ge(y_done, n + 1)
                sp.dma_start(place(out, b, half, ot), y[:, ot % 2, :]).then_inc(y_out[ot % 2], 16)

            def load_a(n, b, half, kt, to=a_of, loaded=a_in):
                wait(sp, kt_done, n * KT + kt + 1)
                sp.dma_start(f32(to[kt]), o_dram[:, bass.ds(b * C + kt * P, P), half * BANK:(half + 1) * BANK]
                             .rearrange("s p n -> p s n")).then_inc(loaded[kt], 16)

            def load_x(b, half, ot):
                r = ot % 2
                before = b * (HEADS // 2) + (half * (KT // 2) + ot // 2)
                wait(sp, y_out[r], 16 * before)
                sp.dma_start(y[:, r, :], place(x, b, half, ot)).then_inc(x_in[r], 16)

            def spread(g):
                sp.wait_ge(recip_done, g + 1)
                sp.dma_start(recip_dram[0], recip[:]).then_inc(recip_out, 16)
                sp.wait_ge(recip_out, 16 * (g + 1))
                sp.dma_start(recip_all[:], recip_dram[0:1].rearrange("a p t -> a (p t)").broadcast_to([DH, N])).then_inc(recip_in, 16)

            def store_head(g):
                ch = bass.ds(g * DH, DH)
                sp.wait_ge(o_hi_done, g + 1)
                sp.dma_start(o_dram[0, ch, :], f32(o_hi[:])).then_inc(o_out, 16)
                sp.wait_ge(o_lo_done, g + 1)
                sp.dma_start(o_dram[1, ch, :], f32(o_lo[:])).then_inc(o_out, 16)

            load(0, 0, 0)
            load(1, 1, 0)
            sp.wait_ge(set_done, SETS)
            maxima(0, 0)
            for part in range(2):
                sp.dma_start(f32(wp[:, part, :, :]), wp_dram[part].rearrange("(k p) o -> p k o", p=P)).then_inc(wp_in, 16)
            for hb in range(HEADS):
                head(hb, hb % BODY, 0, hb)
            head(HEADS, 0, 1, 0)
            for hb in range(1, HEADS):
                head(HEADS + hb, hb % BODY, 1, hb)
            with sp.Fori(2, B - 1) as b:
                for hb in range(HEADS):
                    head(b * HEADS + hb, hb % BODY, b, hb)
            for hb in range(HEADS):
                head((B - 1) * HEADS + hb, hb % BODY, B - 1, hb)
            spread(NH - 2)
            store_group(NH - LAG - 1, *where(B, -1))
            load_x(*where(B, 0))
            store_head(NH - 3)
            sp.wait_ge(s_ready, NH * MT * 2)
            sp.wait_ge(o_out, (NH - 2) * 32)
            for kt in range(KT - 1):
                load_a(-LAG, B - 1, 0, kt, a_last, a_last_in)
                if kt == 0:
                    sp.wait_ge(o_done, NH - 1)
                    spread(NH - 1)
                if kt == 2:
                    store_head(NH - 2)
            for hb in range(1, LAG):
                if hb == LAG - HEADS:
                    store_head(NH - 1)
                    sp.wait_ge(o_out, NH * 32)
                    load_a(-LAG, B - 1, 0, KT - 1, a_last, a_last_in)
                store_group(NH + hb - LAG - 1, *where(B, hb - 1))
                load_x(*where(B, hb))
                if hb == LAG - HEADS:
                    for kt in range(KT):
                        load_a(NH - HEADS - 1, B - 1, 1, kt)
            store_group(NH - 1, *where(B, LAG - 1))
            for r in range(2):
                sp.wait_ge(y_out[r], 16 * NH // 2)

        @block.gpsimd
        def _(pool):
            def add(g, e, t):
                if t == 1:
                    wait(pool, sums_ready, g - SLOTS + 1)
                pool.wait_ge(exp_done, (g * MT + t + 1) * 2)
                if t > 1:
                    pool.wait_ge(added, g * (MT - 1) + t - 1)
                if t == DIVIDE_AT + 1:
                    wait(pool, o_done, g - 1)
                first = p_all[:, exps(e, 0), :] if t == 1 else sums[:, e, :]
                pool.tensor_tensor(sums[:, e, :], first, p_all[:, exps(e, t), :], ALU.add).then_inc(added, 1)

            def divide(g, m, adds):
                pool.wait_ge(added, adds)
                pool.wait_ge(recip_in, 16 * (g + 1))
                pool.wait_ge(un_done, g + 1)
                pool.tensor_tensor(o[:, m % 2, :], o[:, m % 2, :], recip_all[:], ALU.mult).then_inc(o_done, 1)

            def head(g, m, groups, u=None):
                for t in range(1, MT):
                    add(g, m % SLOTS, t)
                    if t == DIVIDE_AT and not (known(g) and g < 2):
                        divide(g - 2, m, g * (MT - 1) + t)

            all_heads(pool, head)
            divide(NH - 2, NH - 2, NH * (MT - 1))
            divide(NH - 1, NH - 1, NH * (MT - 1))

        @block.tensor
        def _(pe):
            PRODUCTS = [(kt, wpart, apart) for kt in range(KT) for wpart, apart in ((0, 0), (0, 1), (1, 0))]

            def scores_by_query(g, e, t, count, to=rows, taken=None):
                if count is not None:
                    pe.wait_ge(qk_in[e], 96 * count)
                    wait(pe, recip_done, g - 2)
                wait(pe, max_done, g * MT + t if taken is None else taken)
                queries = q[:, e, :].rearrange("p (n t) -> p t n", t=MT)[:, t, :]
                for h in range(2):
                    mm = pe.matmul(to[:, h * BANK:(h + 1) * BANK], queries, k[:, e, h * BANK:(h + 1) * BANK],
                                   start=True, stop=True)
                mm.then_inc(rows_ready, 1)

            def scores_by_key(g, e, t):
                if t == 0:
                    pe.wait_ge(max_in, 16 * (g + 1))
                for h in range(2):
                    n = (g * MT + t) * 2 + h
                    r = ((e * MT + t) * 2 + h) % RING
                    cols, keys = slice(h * BANK, (h + 1) * BANK), slice(t * P, (t + 1) * P)
                    wait(pe, exp_done, n - RING + 1)
                    pe.matmul(scores[:, r, :], k[:, e, keys], q[:, e, cols], start=True, stop=False)
                    pe.matmul(scores[:, r, :], k_m[:, e, keys], q_m[:, e, cols], start=False,
                              stop=True).then_inc(s_ready, 1)

            def values(g, e, t, count=None, beside=None):
                pe.wait_ge(lo_done, g * MT + t + 1)
                if t == 0:
                    wait(pe, un_done, g)
                    pe.wait_ge(v_in[e], 16 * count)
                r = t % PARTS
                for h in range(2):
                    cols = slice(h * BANK, (h + 1) * BANK)
                    pe.matmul(heads[:, cols], v[:, e, t, :], p_hi[:, r, cols], start=(t == 0), stop=False)
                    if beside:
                        beside(2 * h)
                    mm = pe.matmul(heads[:, cols], v[:, e, t, :], p_lo[:, r, cols], start=False, stop=(t == MT - 1))
                    if h == 1:
                        mm.then_inc(pv_done, 1)
                    if beside:
                        beside(2 * h + 1)

            def add_up(g, e, t, maxima):
                if t == 0:
                    pe.wait_ge(added, (g + 1) * (MT - 1))
                    pe.wait_ge(max_done, maxima)
                queries = sums[:, e, :].rearrange("p (n t) -> p t n", t=MT)[:, t, :]
                mm = pe.matmul(rows[:, t:t + 1], queries, one[:, 0:1], start=True, stop=True)
                if t == MT - 1:
                    mm.then_inc(sums_ready, 1)

            def output(bank, ot, products, count, beside=None, of=a_of, loaded=a_in):
                for i, (kt, wpart, apart) in enumerate(products):
                    first = (kt, wpart, apart) == PRODUCTS[0]
                    final = (kt, wpart, apart) == PRODUCTS[-1]
                    if ot == 0 and (wpart, apart) == (0, 0):
                        pe.wait_ge(loaded[kt], 16 * count)
                    mm = pe.matmul(bank, wp[:, wpart, kt, ot * P:(ot + 1) * P], of[kt][:, apart, :], start=first, stop=final)
                    if wpart:
                        mm.then_inc(kt_done, 1)
                    if beside:
                        beside(i)

            for t in range(MT):
                scores_by_query(0, 0, t, 1 if t == 0 else None, to=heads if t % 2 else rows, taken=t - 1)
            pe.wait_ge(set_done, SETS)

            HELD = 2

            def head(g, m, groups, u=None):
                e, nxt, prev = m % SLOTS, (m + 1) % SLOTS, (m - 1) % SLOTS
                first, last = known(g) and g == 0, known(g) and g == NH - 1
                for t in range(MT):
                    if not last and t == MT - 1:
                        scores_by_query(g + 1, nxt, t, None)
                    scores_by_key(g, e, t)
                    if not last and t < MT - 1:
                        scores_by_query(g + 1, nxt, t, turn(g + 1, SLOTS, u, m + 1) + 1 if t == 0 else None)
                    if t < 2 and not first:
                        values(g - 1, prev, MT - 2 + t)
                    beside = beside_out = None
                    if t == MT - 1 and not first:
                        at = (g + 1 if last else g + 2) * MT
                        beside = lambda i: i < HELD or add_up(g - 1, prev, i - HELD, at)
                    if t == 3:
                        values(g, e, 0, turn(g, SLOTS, u, m) + 1)
                    if t > 2:
                        values(g, e, t - 2, beside=beside)
                    done = 4 - HELD if beside else 0
                    if groups and OUT_BY_STEP[t]:
                        if t == 0:
                            wait(pe, y_done, g - LAG)
                            if known(g) and g == LAG:
                                pe.wait_ge(wp_in, 32)
                        i = sum(OUT_BY_STEP[:t])
                        output(small, (m - LAG) % BODY, PRODUCTS[i:i + OUT_BY_STEP[t]],
                               turn(g, KT, u, m) - LAG // KT + 1,
                               beside=(lambda i: add_up(g - 1, prev, 4 - HELD + i, at)) if beside else None)
                        done += OUT_BY_STEP[t]
                    if beside:
                        for i in range(done, MT):
                            add_up(g - 1, prev, i, at)

            all_heads(pe, head)
            values(NH - 1, (NH - 1) % SLOTS, MT - 2)
            values(NH - 1, (NH - 1) % SLOTS, MT - 1)
            pe.wait_ge(recip_done, NH - 1)
            for t in range(MT):
                add_up(NH - 1, (NH - 1) % SLOTS, t, NH * MT)
            for n in range(NH - LAG, NH):
                wait(pe, y_done, n - 1 if n > NH - LAG else n)
                bank = psum[:, 7 if n % 2 else 0, :]
                if NH - HEADS <= n < NH - KT:
                    output(bank, n % KT, PRODUCTS, 1, of=a_last, loaded=a_last_in)
                else:
                    output(bank, n % KT, PRODUCTS, n // KT + 1 if n < NH - HEADS else n // KT)

        @block.scalar
        def _(act):
            def take_low(g, m):
                act.wait_ge(pv_done, (g + 1) * MT)
                wait(act, o_hi_done, g - 1)
                wait(act, o_lo_done, g - 1)
                act.copy(o[:, m % 2, :], heads[DH:P, :]).then_inc(low_done, 1)

            def high_out(g, m):
                act.wait_ge(o_done, g + 1)
                wait(act, o_out, 32 * g)
                act.copy(o_hi[:], o[:, m % 2, :]).then_inc(o_hi_done, 1)

            def head(g, m, groups, u=None):
                for t in range(MT):
                    n = g * MT + t
                    if t == 2 and not (known(g) and g == 0):
                        take_low(g - 1, m - 1)
                    back = t - EXPS
                    wait(act, added, g * (MT - 1) + (max(back, 1) if back >= 0 else back + 1))
                    wait(act, lo_done, n - EXPS + 1)
                    for h in range(2):
                        r = ((m % SLOTS * MT + t) * 2 + h) % RING
                        act.wait_ge(s_ready, 2 * n + h + 1)
                        act.activation(p_all[:, exps(m % SLOTS, t), h * BANK:(h + 1) * BANK], scores[:, r, :], ACT.Exp,
                                       scale=SCALE).then_inc(exp_done, 1)
                    act.wait_ge(exp_done, 2 * n + 2)
                    wait(act, pv_done, n - PARTS + 1)
                    act.copy(p_hi[:, t % PARTS, :], p_all[:, exps(m % SLOTS, t), :]).then_inc(hi_done, 1)
                    if t == HIGH_AT and not (known(g) and g < 2):
                        high_out(g - 2, m)

            all_heads(act, head)
            take_low(NH - 1, NH - 1)
            high_out(NH - 2, NH - 2)
            high_out(NH - 1, NH - 1)

        @block.vector
        def _(dve):
            def row_max(g, e, t, of=rows):
                dve.wait_ge(rows_ready, g * MT + t + 1)
                if t == 0:
                    wait(dve, max_in, 16 * (g - SLOTS + 1))
                dve.tensor_reduce(neg_max[:, e, t:t + 1], of, AX.X, ALU.max, negate=True).then_inc(max_done, 1)

            def low_part(g, e, t):
                n = g * MT + t
                dve.wait_ge(hi_done, n + 1)
                dve.tensor_tensor(p_lo[:, t % PARTS, :], p_all[:, exps(e, t), :], f32(p_hi[:, t % PARTS, :]),
                                  ALU.subtract).then_inc(lo_done, 1)

            def take_head(g, m):
                dve.wait_ge(low_done, g + 1)
                dve.tensor_tensor(o[:, m % 2, :], heads[0:DH, :], o[:, m % 2, :], ALU.add).then_inc(un_done, 1)

            def low_out(g, m):
                dve.wait_ge(o_hi_done, g + 1)
                wait(dve, o_out, 32 * g)
                dve.tensor_tensor(o_lo[:], o[:, m % 2, :], f32(o_hi[:]), ALU.subtract).then_inc(o_lo_done, 1)

            def reciprocals(g):
                dve.wait_ge(sums_ready, g + 1)
                wait(dve, recip_out, 16 * g)
                dve.reciprocal(recip[:], rows[:, 0:MT]).then_inc(recip_done, 1)

            def add_x(n, r, count, bank=small):
                dve.wait_ge(kt_done, (n + 1) * KT)
                dve.wait_ge(x_in[r], 16 * count)
                dve.tensor_tensor(y[:, r, :], bank, y[:, r, :], ALU.add).then_inc(y_done, 1)

            dve.memset(one[:], 1.0).then_inc(set_done, 1)
            for e in range(SLOTS):
                dve.memset(f32(q_m[DH:P, e, :]), 0.0).then_inc(set_done, 1)
                dve.memset(f32(k_m[DH:P, e, :]), 0.0).then_inc(set_done, 1)
            dve.wait_ge(set_done, 1 + 2 * SLOTS)
            for e in range(SLOTS):
                dve.memset(f32(k_m[DH:DH + 1, e, :]), 1.0).then_inc(set_done, 1)

            for t in range(MT):
                row_max(0, 0, t, heads if t % 2 else rows)

            def head(g, m, groups, u=None):
                e, nxt = m % SLOTS, (m + 1) % SLOTS
                first, last = known(g) and g == 0, known(g) and g == NH - 1
                for t in range(MT):
                    if t == 2 and not first:
                        take_head(g - 1, m - 1)
                    if not last:
                        row_max(g + 1, nxt, t)
                    if t == MT - 1 and not (known(g) and g < 2):
                        low_out(g - 2, m)
                    low_part(g, e, t)
                if not first:
                    reciprocals(g - 1)
                if groups:
                    add_x(g - LAG, (m - LAG) % 2, (g - LAG) // 2 + 1 if u is None else u * (BODY // 2) + ((m - LAG) // 2 + 1))

            all_heads(dve, head)
            take_head(NH - 1, NH - 1)
            reciprocals(NH - 1)
            for n in range(NH - LAG, NH):
                add_x(n, n % 2, n // 2 + 1, psum[:, 7 if n % 2 else 0, :])
                if n == NH - LAG:
                    low_out(NH - 2, NH - 2)
                if n == NH - LAG + 1:
                    low_out(NH - 1, NH - 1)


def build(nc, x, wq, wk, wv, wp, ident_in, avg_in, scratch, out):
    S = Shapes(x)
    assert S.C % P == 0 and S.N == 2 * BANK and 2 * S.DH == P and (S.C // GROUPS) % S.KT == 0
    q_dram, k_dram, v_dram, o_dram, wp_dram, recip_dram = scratch
    with nc.psum_tensor("psum", [P, 8, BANK], F32) as psum:
        project_phase(nc, S, x, (wp, wq, wk, wv), ident_in, avg_in, wp_dram, q_dram, k_dram, v_dram, psum)
        attend_phase(nc, S, x, wp_dram, q_dram, k_dram, v_dram, o_dram, recip_dram, out, psum)


def kernel(x, L0_conv_Wq, L0_conv_Wk, L0_conv_Wv, L0_conv_Wp):
    import numpy as np
    import concourse.bacc as bacc
    from concourse.bass_utils import run_bass_kernel_spmd

    nc = bacc.Bacc("TRN2", target_bir_lowering=False, num_devices=1)
    Bn, Cn, Hn, Wn = x.shape
    Nn, Dn = Hn * Wn, Cn // HEADS
    per_group = Cn // GROUPS // (Cn // P)
    arrays = {
        "x": np.ascontiguousarray(x).reshape(Bn, Cn, Nn),
        "wq": np.ascontiguousarray(L0_conv_Wq), "wk": np.ascontiguousarray(L0_conv_Wk),
        "wv": np.ascontiguousarray(L0_conv_Wv), "wp": np.ascontiguousarray(L0_conv_Wp),
        "ident": np.eye(P, dtype=np.float32),
        "avg": np.kron(np.eye(P // per_group), np.full((per_group, per_group), 1.0 / per_group)).astype(np.float32),
    }
    args = [nc.dram_tensor("in_" + n, a.shape, F32, kind="ExternalInput").ap() for n, a in arrays.items()]
    shapes = {
        "q_parts": (2, Bn * Cn, Nn), "k_parts": (2, Bn * Cn, Nn), "v_parts": (Bn * HEADS, P, Nn // P, 2 * Dn),
        "o_parts": (2, Bn * Cn, Nn), "wp_parts": (2, Cn, Cn), "recip_rows": (2, P, Nn // P),
    }
    scratch = [nc.dram_tensor(n, s, F32, kind="Internal").ap() for n, s in shapes.items()]
    out = nc.dram_tensor("out", (Bn, Cn, Nn), F32, kind="ExternalOutput").ap()
    build(nc, *args, scratch, out)
    got = run_bass_kernel_spmd(nc, [{"in_" + n: a for n, a in arrays.items()}], core_ids=[0])
    return got.results[0]["out"].reshape(Bn, Cn, Hn, Wn)
```
